# Optimizing a Trainium2 kernel written in Bass

```python
import numpy as np
import jax
import jax.numpy as jnp

def _softmax(x, axis=-1):
    return jax.nn.softmax(x, axis=axis)

def _gelu(x):
    return jax.nn.gelu(x, approximate=True)

def _silu(x):
    return jax.nn.silu(x)

def _sigmoid(x):
    return jax.nn.sigmoid(x)

def _layernorm(x, axis=-1, eps=1e-05):
    m = jnp.mean(x, axis=axis, keepdims=True)
    v = jnp.var(x, axis=axis, keepdims=True)
    return (x - m) / jnp.sqrt(v + eps)

def _scatter_add(tgt, idx, src, axis=0):
    return tgt.at[idx].add(src)

def _segment_sum(src, seg, n):
    return jax.ops.segment_sum(src, seg, n)
kernel_name = 'mk_gnn_resnorm_d2_gnn_r8_038a54'

def setup_inputs(seed: int=0):
    np.random.seed(seed)
    _w = jnp.asarray

    def _rec_inputs():
        import jax
        import jax.numpy as jnp
        _gk = jax.random.key(seed)
        x = -0.000202 + 1 * jax.random.normal(jax.random.fold_in(_gk, 1), (6250, 128), jnp.float32)
        src = jax.random.randint(jax.random.fold_in(_gk, 2), (200000,), 0, 6250, jnp.int32)
        dst = jax.random.randint(jax.random.fold_in(_gk, 3), (200000,), 0, 6250, jnp.int32)
        _o = jnp.argsort(dst, stable=True)
        src = src[_o]
        dst = dst[_o]
        edge_attr_4 = -0.000107899 + 1.00008 * jax.random.normal(jax.random.fold_in(_gk, 11), (200000, 4), jnp.float32)
        edge_attr_8 = jax.random.uniform(jax.random.fold_in(_gk, 12), (200000, 8), jnp.float32, 0.0, 1)
        return (x, src, dst, edge_attr_4, edge_attr_8)
    x, src, dst, edge_attr_4, edge_attr_8 = _rec_inputs()

    def _L0_gnn_setup():
        import jax, jax.numpy as jnp
        import numpy as np
        MUL = 32
        N_NODES = 6250
        N_EDGES = 100000
        R3 = np.sqrt(3.0).astype(np.float32)
        key = jax.random.key(seed)
        ks = jax.random.split(key, 12)
        inp = {}
        inp['node_feats'] = jax.random.normal(ks[0], (N_NODES, 4 * MUL), dtype=jnp.float32)
        inp['edge_attrs'] = jax.random.normal(ks[1], (N_EDGES, 4), dtype=jnp.float32)
        inp['edge_feats'] = jax.random.uniform(ks[2], (N_EDGES, 8), dtype=jnp.float32)
        inp['edge_index'] = jax.random.randint(ks[3], (2, N_EDGES), 0, N_NODES)
        inp['W_up_s'] = jax.random.normal(ks[4], (MUL, MUL), dtype=jnp.float32)
        inp['W_up_v'] = jax.random.normal(ks[5], (MUL, MUL), dtype=jnp.float32)
        inp['A1'] = jax.random.normal(ks[6], (8, 64), dtype=jnp.float32) / np.sqrt(8.0)
        inp['b1'] = jnp.zeros((64,), dtype=jnp.float32)
        inp['A2'] = jax.random.normal(ks[7], (64, 64), dtype=jnp.float32) / np.sqrt(64.0)
        inp['b2'] = jnp.zeros((64,), dtype=jnp.float32)
        inp['A3'] = jax.random.normal(ks[8], (64, 4 * MUL), dtype=jnp.float32) * (10.0 * np.sqrt(6.0 / (64 + 4 * MUL)))
        inp['W_out_s'] = jax.random.normal(ks[9], (2 * MUL, MUL), dtype=jnp.float32)
        inp['W_out_v'] = jax.random.normal(ks[10], (2 * MUL, MUL), dtype=jnp.float32)
        return inp
    _L0_gnn_all = _L0_gnn_setup()
    _L0_gnn_in = {k: v for k, v in _L0_gnn_all.items() if k in ('W_up_s', 'W_up_v', 'A1', 'b1', 'A2', 'b2', 'A3', 'W_out_s', 'W_out_v')}
    del _L0_gnn_all

    def _L1_gnn_setup():
        import jax, jax.numpy as jnp
        import numpy as np
        N_NODES = 12500
        N_EDGES = 200000
        HIDDEN = 128
        HEADS = 8
        HEAD_DIM = HIDDEN // HEADS
        ALPHA = 0.2
        LN_EPS = 1e-05

        def _gat_forward(x, edge_index, W, a, ln_gamma, ln_beta):
            n = x.shape[0]
            row, col = (edge_index[0], edge_index[1])
            x_heads = jnp.einsum('ni,hij->nhj', x, W)
            a_vec = a[..., 0]
            a_i, a_j = (a_vec[:, :HEAD_DIM], a_vec[:, HEAD_DIM:])
            s_i = jnp.einsum('nhd,hd->nh', x_heads, a_i)
            s_j = jnp.einsum('nhd,hd->nh', x_heads, a_j)
            e = s_i[row] + s_j[col]
            e = jnp.where(e >= 0, e, ALPHA * e)
            m = jax.ops.segment_max(e, row, num_segments=n)
            m = jnp.where(jnp.isfinite(m), m, 0.0)
            ex = jnp.exp(e - m[row])
            denom = jax.ops.segment_sum(ex, row, num_segments=n)
            attn = ex / denom[row]
            weighted = x_heads[row] * attn[..., None]
            out_heads = jax.ops.segment_sum(weighted, col, num_segments=n)
            out = out_heads.reshape(n, HIDDEN)
            out = out + x
            mu = jnp.mean(out, axis=-1, keepdims=True)
            var = jnp.mean(jnp.square(out - mu), axis=-1, keepdims=True)
            out = (out - mu) * jax.lax.rsqrt(var + LN_EPS)
            return out * ln_gamma + ln_beta
        key = jax.random.key(seed)
        k1, k2, k3, k4 = jax.random.split(key, 4)
        x = jax.random.normal(k1, (N_NODES, HIDDEN), dtype=jnp.float32)
        edge_index = jax.random.randint(k2, (2, N_EDGES), 0, N_NODES, dtype=jnp.int64)
        w_bound = np.sqrt(6.0 / (HIDDEN + HEAD_DIM))
        a_bound = np.sqrt(6.0 / (2 * HEAD_DIM + 1))
        W = jax.random.uniform(k3, (HEADS, HIDDEN, HEAD_DIM), minval=-w_bound, maxval=w_bound, dtype=jnp.float32)
        a = jax.random.uniform(k4, (HEADS, 2 * HEAD_DIM, 1), minval=-a_bound, maxval=a_bound, dtype=jnp.float32)
        ln_gamma = jnp.ones((HIDDEN,), dtype=jnp.float32)
        ln_beta = jnp.zeros((HIDDEN,), dtype=jnp.float32)
        return {'x': x, 'edge_index': edge_index, 'W': W, 'a': a, 'ln_gamma': ln_gamma, 'ln_beta': ln_beta}
    _L1_gnn_all = _L1_gnn_setup()
    _L1_gnn_in = {k: v for k, v in _L1_gnn_all.items() if k in ('W', 'a', 'ln_gamma', 'ln_beta')}
    del _L1_gnn_all
    return {'x': x, 'src': src, 'dst': dst, 'edge_attr_4': edge_attr_4, 'edge_attr_8': edge_attr_8, 'L0_gnn_W_up_s': _L0_gnn_in['W_up_s'], 'L0_gnn_W_up_v': _L0_gnn_in['W_up_v'], 'L0_gnn_A1': _L0_gnn_in['A1'], 'L0_gnn_b1': _L0_gnn_in['b1'], 'L0_gnn_A2': _L0_gnn_in['A2'], 'L0_gnn_b2': _L0_gnn_in['b2'], 'L0_gnn_A3': _L0_gnn_in['A3'], 'L0_gnn_W_out_s': _L0_gnn_in['W_out_s'], 'L0_gnn_W_out_v': _L0_gnn_in['W_out_v'], 'L1_gnn_W': _L1_gnn_in['W'], 'L1_gnn_a': _L1_gnn_in['a'], 'L1_gnn_ln_gamma': _L1_gnn_in['ln_gamma'], 'L1_gnn_ln_beta': _L1_gnn_in['ln_beta']}

def reference(x, src, dst, edge_attr_4, edge_attr_8, L0_gnn_W_up_s, L0_gnn_W_up_v, L0_gnn_A1, L0_gnn_b1, L0_gnn_A2, L0_gnn_b2, L0_gnn_A3, L0_gnn_W_out_s, L0_gnn_W_out_v, L1_gnn_W, L1_gnn_a, L1_gnn_ln_gamma, L1_gnn_ln_beta):
    import jax
    import jax.numpy as jnp

    def _L0_gnn_ref(node_feats, edge_attrs, edge_feats, W_up_s, W_up_v, A1, b1, A2, b2, A3, W_out_s, W_out_v, edge_index):
        import jax, jax.numpy as jnp
        import numpy as np
        MUL = 32
        N_NODES = 6250
        N_EDGES = 100000
        R3 = np.sqrt(3.0).astype(np.float32)
        num_nodes = node_feats.shape[0]
        sender, receiver = (edge_index[0], edge_index[1])
        s = node_feats[:, :MUL]
        v = node_feats[:, MUL:].reshape(num_nodes, MUL, 3)
        inv = 1.0 / np.sqrt(MUL).astype(np.float32)
        s = s @ W_up_s * inv
        v = jnp.einsum('nui,uw->nwi', v, W_up_v) * inv
        h = jax.nn.silu(edge_feats @ A1 + b1)
        h = jax.nn.silu(h @ A2 + b2)
        tpw = h @ A3
        w0, w1, w2, w3 = jnp.split(tpw, 4, axis=1)
        ss = s[sender]
        vs = v[sender]
        y_s = edge_attrs[:, :1]
        y_v = edge_attrs[:, 1:4]
        out_s0 = ss * y_s * w0
        out_s3 = jnp.einsum('eui,ei->eu', vs, y_v) / R3 * w3
        out_v1 = ss[:, :, None] * y_v[:, None, :] * w1[:, :, None]
        out_v2 = vs * y_s[:, :, None] * w2[:, :, None]
        E = ss.shape[0]
        mji = jnp.concatenate([out_s0, out_s3, out_v1.reshape(E, 3 * MUL), out_v2.reshape(E, 3 * MUL)], axis=1)
        message = jax.ops.segment_sum(mji, receiver, num_segments=num_nodes) / 10.0
        ms = message[:, :2 * MUL]
        mv = message[:, 2 * MUL:].reshape(num_nodes, 2 * MUL, 3)
        inv2 = 1.0 / np.sqrt(2 * MUL).astype(np.float32)
        out_s = ms @ W_out_s * inv2
        out_v = jnp.einsum('nui,uw->nwi', mv, W_out_v) * inv2
        return jnp.concatenate([out_s, out_v.reshape(num_nodes, 3 * MUL)], axis=1)

    def _L1_gnn_ref(x, edge_index, W, a, ln_gamma, ln_beta):
        import jax, jax.numpy as jnp
        import numpy as np
        N_NODES = 12500
        N_EDGES = 200000
        HIDDEN = 128
        HEADS = 8
        HEAD_DIM = HIDDEN // HEADS
        ALPHA = 0.2
        LN_EPS = 1e-05

        def _gat_forward(x, edge_index, W, a, ln_gamma, ln_beta):
            n = x.shape[0]
            row, col = (edge_index[0], edge_index[1])
            x_heads = jnp.einsum('ni,hij->nhj', x, W)
            a_vec = a[..., 0]
            a_i, a_j = (a_vec[:, :HEAD_DIM], a_vec[:, HEAD_DIM:])
            s_i = jnp.einsum('nhd,hd->nh', x_heads, a_i)
            s_j = jnp.einsum('nhd,hd->nh', x_heads, a_j)
            e = s_i[row] + s_j[col]
            e = jnp.where(e >= 0, e, ALPHA * e)
            m = jax.ops.segment_max(e, row, num_segments=n)
            m = jnp.where(jnp.isfinite(m), m, 0.0)
            ex = jnp.exp(e - m[row])
            denom = jax.ops.segment_sum(ex, row, num_segments=n)
            attn = ex / denom[row]
            weighted = x_heads[row] * attn[..., None]
            out_heads = jax.ops.segment_sum(weighted, col, num_segments=n)
            out = out_heads.reshape(n, HIDDEN)
            out = out + x
            mu = jnp.mean(out, axis=-1, keepdims=True)
            var = jnp.mean(jnp.square(out - mu), axis=-1, keepdims=True)
            out = (out - mu) * jax.lax.rsqrt(var + LN_EPS)
            return out * ln_gamma + ln_beta
        return _gat_forward(x, edge_index, W, a, ln_gamma, ln_beta)
    edge_index = jnp.stack([src, dst])
    x = _layernorm(x + _L0_gnn_ref(x, edge_attr_4, edge_attr_8, L0_gnn_W_up_s, L0_gnn_W_up_v, L0_gnn_A1, L0_gnn_b1, L0_gnn_A2, L0_gnn_b2, L0_gnn_A3, L0_gnn_W_out_s, L0_gnn_W_out_v, edge_index), axis=-1)
    x = _layernorm(x + _L1_gnn_ref(x, edge_index, L1_gnn_W, L1_gnn_a, L1_gnn_ln_gamma, L1_gnn_ln_beta), axis=-1)
    return x

_drawn_inputs = setup_inputs


def setup_inputs(seed=0):
    import zlib

    import numpy as np

    out = dict(_drawn_inputs(seed))
    spreads = {'L0_gnn_b1': (0.0, 0.1),
     'L0_gnn_b2': (0.0, 0.1),
     'L1_gnn_ln_gamma': (1.0, 0.2),
     'L1_gnn_ln_beta': (0.0, 0.1)}
    factors = {}
    for name, (base, spread) in spreads.items():
        noise = np.random.default_rng([zlib.crc32(name.encode()), seed]).standard_normal(out[name].shape)
        drawn = base * np.exp(spread * noise) if base else spread * noise
        out[name] = jnp.asarray(drawn.astype(out[name].dtype))
    for name, factor in factors.items():
        out[name] = (out[name] * factor).astype(out[name].dtype)
    return out
```

```python
from contextlib import ExitStack

import concourse.bass as bass
from concourse import mybir

F32 = mybir.dt.float32
I32 = mybir.dt.int32
I16 = mybir.dt.int16
ALU = mybir.AluOpType
ACT = mybir.ActivationFunctionType
AX = mybir.AxisListType

P = 128
N_NODES, D = 6250, 128
MUL, HID, EF = 32, 64, 8
HEADS, HD = 8, 16
NB = -(-N_NODES // P)
NP = NB * P
CB = 7
NCH = NB // CB
CN = CB * P
TG = 4
GE = TG * P
N_EDGES = 200000
U = 4
NG = -(-N_EDGES // (GE * U)) * U
T = NG * TG
HG = GE // 2
W = 32
NW = NP + W
TP = 98
TQ = NG // TP
EPS = 1e-5
ALPHA = 0.2
INV_UP = float(MUL) ** -0.5
INV_OUT = (2.0 * MUL) ** -0.5 / 10.0
INV_R3 = 3.0 ** -0.5
NU = NG // U
XW = D + 2 * HEADS
XMAX = NG * (NP // W)


def build(nc, x_t, x_n, src_t, src_g, dst_t, dst_f, y_t, ea_t, w_up_s, w_up_v, a1, b1, a2, b2, a3,
          w_out_s, w_out_v, w_att, a_att, gamma, beta, out, up_tab, x1_tab, score_tab, sj_tab,
          xh_tab, range_tab):
    with ExitStack() as ctx:
        def sb(name, shape, dt=F32):
            return ctx.enter_context(nc.sbuf_tensor(name, shape, dt))

        def sem(name):
            return ctx.enter_context(nc.semaphore(name))

        ident = sb("ident", [P, P])
        iota_n = sb("iota_n", [P, NW], I16)
        p_col = sb("p_col", [P, 1], I16)
        dst_sb = sb("dst_sb", [P, T])
        tile_i = sb("tile_i", [P, T], I32)
        acc = sb("acc", [P, 4 * NW])
        acc0 = acc[:, :].rearrange("p (c n) -> p c n", c=4)
        at = [0]

        def part(n):
            at[0] += n
            return acc[:, at[0] - n:at[0]]

        ex = part(T * HEADS).rearrange("p (t h) -> p t h", h=HEADS)
        acc1 = part(NW)
        src_lo = part(T)
        src_hi = part(T)
        hist_flat = part(2 * TG * NB * HEADS)
        hist_rhs = hist_flat.rearrange("p (s k b h) -> p s k b h", s=2, k=TG, h=HEADS)
        assert at[0] <= 4 * NW and 2 * TG * NB * HEADS >= 2 * T
        int_lo = hist_flat[:, 0:T].bitcast(I32)
        int_hi = hist_flat[:, T:2 * T].bitcast(I32)
        yx = sb("yx", [P, T * 4])
        y_sb = yx[:, :].rearrange("p (t c) -> p t c", c=4)
        xh = yx[:, 0:NB * D].rearrange("p (b f) -> p b f", f=D)
        w_up = sb("w_up", [P, D])
        a1_sb = sb("a1_sb", [2 * EF, P])
        a2_sb = sb("a2_sb", [P, P])
        a3_sb = sb("a3_sb", [P, 2 * P])
        b1_sb = sb("b1_sb", [P, 1])
        b2_sb = sb("b2_sb", [P, 1])
        w_out = sb("w_out", [P, 4, D])
        w_cat = sb("w_cat", [P, D + 2 * HEADS])
        a_bc = sb("a_bc", [P, HEADS, 2 * HD])
        gamma_bc = sb("gamma_bc", [P, D])
        beta_bc = sb("beta_bc", [P, D])
        g_tab = sb("g_tab", [1, 2, NG + 1], I32)
        idx = sb("idx", [P, U, TG], I32)
        ea = sb("ea", [2 * EF, U, HG])
        rows = sb("rows", [P, U, TG, D])
        rows_flat = rows[:, :, :, :].rearrange("p u k f -> p (u k f)")
        scratch = rows_flat[:, 0:CN].rearrange("p (b f) -> p b f", f=D)
        dst_row = rows_flat[0:W, :].bitcast(I32).rearrange("p (u e) -> p u e", u=U)
        h1 = sb("h1", [P, 2, HG])
        h2 = sb("h2", [P, 2, HG])
        prod = sb("prod", [P, 2, TG, 2, D])
        lo_hot = prod[:, :, :, 0, :]
        weighed = prod[:, :, :, 1, :]
        sel = sb("sel", [P, 2, TG, 4, W])
        sel_t = sel[0:W, :, :, :, :].rearrange("p s k c n -> p s (k c n)")
        rng_i = acc[0:TP, 0:TQ * GE].bitcast(I32).rearrange("p (q e) -> p q e", q=TQ)
        rng_f = sb("rng_f", [TP, 3, TQ])
        rng_o = sb("rng_o", [TP, 2, TQ], I32)
        g_sum = prod[0:1, :, :, :, :].rearrange("p s k q f -> p s (k q f)")[:, :, 0:NG]
        chunk = sb("chunk", [P, CN])
        node_a = sb("node_a", [P, CB, D])
        node_b = sb("node_b", [P, CB, D])
        node_s = sb("node_s", [P, 4, CB])
        score = sb("score", [P, NB, 2 * HEADS])
        shift = sb("shift", [P, NB, 2 * HEADS])
        s_max = sb("s_max", [P, 2, HEADS])
        s_rows = sb("s_rows", [P, U, TG, 2 * HEADS])
        sj_win = sb("sj_win", [W, U, HEADS])
        sj_winx = sb("sj_winx", [W, HEADS])
        z = sb("z", [P, 3, TG, HEADS])
        den = chunk[:, 0:2 * NB * HEADS].rearrange("p (n b h) -> p n b h", n=2, h=HEADS)
        zeros = sb("zeros", [W, HEADS])

        bank = [ctx.enter_context(nc.psum_tensor(f"bank{i}", [P, 512], F32)) for i in range(8)]
        p_h = [bank[i][:, :].rearrange("p (l n) -> p l n", l=2) for i in range(2)]
        p_w = [bank[2 + i][:, :].rearrange("p (k m) -> p k m", k=TG) for i in range(2)]
        p_seg = [bank[4 + i][:, 0:4 * W].rearrange("p (c n) -> p c n", c=4) for i in range(2)]
        p_segx = bank[6][:, 0:4 * W].rearrange("p (c n) -> p c n", c=4)
        p_sj = [bank[4 + i][:, 0:TG * HEADS].rearrange("p (k h) -> p k h", k=TG) for i in range(2)]
        p_sjx = bank[6][:, 0:TG * HEADS].rearrange("p (k h) -> p k h", k=TG)
        p_den = bank[7][:, 0:NB * HEADS]

        def blocks(first, b, width):
            per = 512 // width
            return bank[(first + b // per) % 8][:, b % per * width:(b % per + 1) * width]

        def window(base, x, x0):
            return nc.s_assert_within(base + (x - x0 + 1) * W, 0, NP - 1, 
                                      skip_runtime_bounds_check_because="a window starts at or below the largest dst")

        cleared = sem("cleared")
        consts = sem("consts")
        loaded = sem("loaded")
        dst_loaded = sem("dst_loaded")
        src_loaded = sem("src_loaded")
        tile_free = sem("tile_free")
        prep = sem("prep")
        prep_done = sem("prep_done")
        rng_loaded = sem("rng_loaded")
        rng_ready = sem("rng_ready")
        rng_saved = sem("rng_saved")
        rng_back = sem("rng_back")
        table_ready = sem("table_ready")
        xt_loaded = sem("xt_loaded")
        up_done = sem("up_done")
        up_copied = sem("up_copied")
        up_saved = sem("up_saved")

        idx_ready = [sem(f"idx_ready{u}") for u in range(U)]
        ea_ready = [sem(f"ea_ready{u}") for u in range(U)]
        gathered = [sem(f"gathered{u}") for u in range(U)]
        l1_done = sem("l1_done")
        l2_done = sem("l2_done")
        w_done = sem("w_done")
        h1_ready = sem("h1_ready")
        h2_ready = sem("h2_ready")
        prod_ready = sem("prod_ready")
        seg_done = sem("seg_done")
        summed = sem("summed")
        summedx = sem("summedx")
        selx_ready = sem("selx_ready")
        segx_done = sem("segx_done")
        sums_ready = sem("sums_ready")

        out_t_done = sem("out_t_done")
        out_t_copied = sem("out_t_copied")
        out_done = sem("out_done")
        xn_loaded = sem("xn_loaded")
        node = sem("node")
        var_ready = sem("var_ready")
        std_ready = sem("std_ready")
        x1_ready = sem("x1_ready")
        x1_saved = sem("x1_saved")
        x1_t_done = sem("x1_t_done")
        x1_t_copied = sem("x1_t_copied")
        xh_done = sem("xh_done")
        xh_copied = sem("xh_copied")

        max_ready = sem("max_ready")
        max_all = sem("max_all")
        shift_ready = sem("shift_ready")
        scores_saved = sem("scores_saved")
        row_ready = [sem(f"row_ready{u}") for u in range(U)]
        sj_ready = [sem(f"sj_ready{u}") for u in range(U)]
        sjx_ready = sem("sjx_ready")
        sel_t_ready = sem("sel_t_ready")
        sj_done = sem("sj_done")
        sel_tx_ready = sem("sel_tx_ready")
        sjx_done = sem("sjx_done")
        z_ready = sem("z_ready")
        z_sum = sem("z_sum")
        z_sumx = sem("z_sumx")
        leaky = sem("leaky")
        ex_ready = sem("ex_ready")
        hist_ready = sem("hist_ready")
        hist_done = sem("hist_done")
        hist_zero = sem("hist_zero")
        hist_start = sem("hist_start")
        xh_ready = sem("xh_ready")
        xh_saved = sem("xh_saved")

        weighed_ready = sem("weighed_ready")
        agg_done = sem("agg_done")
        added = sem("added")
        addedx = sem("addedx")
        hotx_ready = sem("hotx_ready")
        aggx_done = sem("aggx_done")
        agg_ready = sem("agg_ready")
        last_copied = sem("last_copied")
        last_done = sem("last_done")
        x1_loaded = sem("x1_loaded")
        last_var = sem("last_var")
        last_std = sem("last_std")
        last = sem("last")
        y_ready = sem("y_ready")
        out_saved = sem("out_saved")

        block = ctx.enter_context(nc.Block())

        N_LOADS = 4 + 2 * 5 + 1 + 3 * 3 + 5
        N_CLEAR = 5

        @block.sync
        def _(sp):
            sp.dma_start(rng_i, dst_f.rearrange("(p q) e -> p q e", q=TQ)).then_inc(rng_loaded, 16)
            sp.dma_start(tile_i[:, :], dst_t).then_inc(dst_loaded, 16)
            sp.wait_ge(cleared, N_CLEAR)
            for c in range(4):
                r = slice(MUL * c, MUL * (c + 1))
                sp.dma_start(w_up[r, r], w_up_s if c == 0 else w_up_v).then_inc(loaded, 16)
            for h in range(2):
                sp.dma_start(a1_sb[EF * h:EF * (h + 1), HID * h:HID * (h + 1)], a1).then_inc(loaded, 16)
                sp.dma_start(a2_sb[HID * h:HID * (h + 1), HID * h:HID * (h + 1)], a2).then_inc(loaded, 16)
                sp.dma_start(a3_sb[HID * h:HID * (h + 1), P * h:P * (h + 1)], a3).then_inc(loaded, 16)
                sp.dma_start(b1_sb[HID * h:HID * (h + 1), :], b1.unsqueeze(1)).then_inc(loaded, 16)
                sp.dma_start(b2_sb[HID * h:HID * (h + 1), :], b2.unsqueeze(1)).then_inc(loaded, 16)
            sp.dma_start(w_out[0:MUL, 0, 0:MUL], w_out_s[0:MUL, :]).then_inc(loaded, 16)
            for i in range(3):
                r = slice(MUL * (1 + i), MUL * (2 + i))
                sp.dma_start(w_out[r, 0, r], w_out_v[MUL:2 * MUL, :]).then_inc(loaded, 16)
                sp.dma_start(w_out[0:MUL, 1 + i, r], w_out_v[0:MUL, :]).then_inc(loaded, 16)
                sp.dma_start(w_out[r, 1 + i, 0:MUL], w_out_s[MUL:2 * MUL, :]).then_inc(loaded, 16)
            sp.dma_start(w_cat[:, 0:D].rearrange("p (h j) -> p h j", h=HEADS),
                         w_att.rearrange("h i j -> i h j")).then_inc(loaded, 16)
            sp.dma_start(a_bc[:, :, :].rearrange("p h j -> p (h j)"), a_att.partition_broadcast(P)).then_inc(loaded, 16)
            sp.dma_start(gamma_bc[:, :], gamma.partition_broadcast(P)).then_inc(loaded, 16)
            sp.dma_start(beta_bc[:, :], beta.partition_broadcast(P)).then_inc(loaded, 16)
            sp.dma_start(yx[:, :], y_t).then_inc(loaded, 16)
            sp.wait_ge(rng_ready, 1)
            sp.dma_start(range_tab.rearrange("r (p q) -> p r q", q=TQ), rng_o[:, :, :]).then_inc(rng_saved, 16)
            sp.wait_ge(rng_saved, 16)
            sp.dma_start(g_tab[0:1, :, 0:NG], range_tab.rearrange("(o r) g -> o r g", o=1)).then_inc(rng_back, 16)
            sp.dma_start(chunk[:, :], x_t[:, 0:CN]).then_inc(xt_loaded, 16)
            with sp.Fori(1, NCH) as c:
                sp.wait_ge(up_done, c)
                sp.dma_start(chunk[:, :], x_t[:, bass.ds(c * CN, CN)]).then_inc(xt_loaded, 16)
            sp.wait_ge(tile_free, 1)
            sp.dma_start(tile_i[:, :], src_t).then_inc(src_loaded, 16)

            def load_idx(g, u):
                sp.dma_start(idx[:, u, :], src_g[bass.ds(g * P, P), :]).then_inc(idx_ready[u], 16)

            for u in range(U):
                load_idx(u, u)
                sp.dma_start(ea[:, u, :], ea_t[:, u * HG:(u + 1) * HG]).then_inc(ea_ready[u], 16)
            with sp.Fori(1, NU) as i:
                for u in range(U):
                    sp.wait_ge(gathered[u], i * (16 * TG))
                    load_idx(i * U + u, u)
                    sp.wait_ge(l1_done, (i - 1) * U + (u + 1))
                    sp.dma_start(ea[:, u, :], ea_t[:, bass.ds((i * U + u) * HG, HG)]).then_inc(ea_ready[u], 16)
            for u in range(2):
                sp.wait_ge(l1_done, NG - U + u + 1)
                sp.dma_start(ea[:, u, :], ea_t[:, (NG + u) * HG:(NG + u + 1) * HG]).then_inc(ea_ready[u], 16)

            sp.dma_start(node_b[:, :, :], x_n[0:CN, :].rearrange("(b p) f -> p b f", p=P)).then_inc(xn_loaded, 16)
            with sp.Fori(0, NCH) as c:
                sp.wait_ge(x1_ready, c + 1)
                sp.dma_start(x1_tab[bass.ds(c * CN, CN), :].rearrange("(b p) f -> p b f", p=P),
                             node_a[:, :, :]).then_inc(x1_saved, 16)
                sp.dma_start(node_b[:, :, :], x_n[bass.ds(c * CN + CN, CN), :].rearrange("(b p) f -> p b f", p=P)
                             ).then_inc(xn_loaded, 16)

            sp.wait_ge(shift_ready, 1)
            sp.dma_start(score_tab.rearrange("(b p) h -> p b h", p=P), shift[:, :, :]).then_inc(scores_saved, 16)
            sp.dma_start(sj_tab[0:NP, :].rearrange("(b p) h -> p b h", p=P), score[:, :, HEADS:]).then_inc(scores_saved, 16)
            sp.dma_start(sj_tab[NP:NW, :], zeros[:, :]).then_inc(scores_saved, 16)
            sp.wait_ge(scores_saved, 48)

            def pass_b(i, first):
                for u in range(U):
                    g = i * U + u
                    sp.wait_ge(gathered[u], (i + NU) * (16 * TG))
                    load_idx(g, u)
                    if not first:
                        sp.wait_ge(z_ready, (i - 1) * U + (u + 1))
                    sp.dma_start(dst_row[:, u, :], dst_f[bass.ds(g, 1), :].squeeze(0).partition_broadcast(W)
                                 ).then_inc(row_ready[u], 16)
                    base = sp.value_load(g_tab[0:1, 0, bass.ds(g, 1)], min_val=0, max_val=NP - 1)
                    sp.dma_start(sj_win[:, u, :], sj_tab[bass.ds(base, W), :]).then_inc(sj_ready[u], 16)
                    x0 = sp.value_load(g_tab[0:1, 1, bass.ds(g, 1)], min_val=0, max_val=XMAX)
                    x1 = sp.value_load(g_tab[0:1, 1, bass.ds(g + 1, 1)], min_val=0, max_val=XMAX)
                    with sp.If(x1 > x0):
                        with sp.Fori(x0, x1) as x:
                            sp.wait_ge(z_sumx, x + 1)
                            sp.dma_start(sj_winx[:, :], sj_tab[bass.ds(window(base, x, x0), W), :]).then_inc(sjx_ready, 16)

            pass_b(0, True)
            with sp.Fori(1, NU) as i:
                pass_b(i, False)

            sp.wait_ge(xh_ready, 1)
            sp.dma_start(xh_tab.rearrange("(b p) f -> p b f", p=P), xh).then_inc(xh_saved, 16)
            with sp.Fori(0, NU) as i:
                for u in range(U):
                    sp.wait_ge(gathered[u], (i + 2 * NU) * (16 * TG))
                    load_idx(i * U + u, u)

            with sp.Fori(0, NCH) as c:
                sp.dma_start(node_b[:, :, :], x1_tab[bass.ds(c * CN, CN), :].rearrange("(b p) f -> p b f", p=P)
                             ).then_inc(x1_loaded, 16)
                sp.wait_ge(y_ready, c + 1)
                sp.dma_start(out[bass.ds(c * CN, CN), :].rearrange("(b p) f -> p b f", p=P),
                             node_a[:, :, :]).then_inc(out_saved, 16)
            sp.wait_ge(out_saved, 16 * NCH)
            sp.wait_ge(xn_loaded, 16 * (NCH + 1))
            sp.wait_ge(x1_saved, 16 * NCH)
            sp.wait_ge(xh_saved, 16)
            sp.wait_ge(up_saved, 16 * NCH)

        @block.gpsimd
        def _(pool):
            pool.memset(ident[:, :], 0.0).then_inc(consts, 1)
            pool.wait_ge(consts, 1)
            pool.affine_select(out=ident[:, :], in_=ident[:, :], compare_op=ALU.not_equal, fill=1.0, base=0,
                               pattern=[[-1, P]], channel_multiplier=1).then_inc(consts, 1)
            pool.iota(iota_n[:, :], pattern=[[1, NW]], base=0, channel_multiplier=0).then_inc(consts, 1)
            pool.iota(p_col[:, :], pattern=[[1, 1]], base=0, channel_multiplier=1).then_inc(consts, 1)

            def gather(table, slots, u):
                for k in range(TG):
                    pool.indirect_dma_start(out=slots[:, u, k, :], out_offset=None, in_=table[:, :],
                                            in_offset=bass.IndirectOffsetOnAxis(ap=idx[:, u, k:k + 1], axis=0)
                                            ).then_inc(gathered[u], 16)

            def gather_pass(turn, table, slots, used):
                for u in range(U):
                    pool.wait_ge(idx_ready[u], turn * NU * 16 + 16)
                    gather(table, slots, u)
                with pool.Fori(1, NU) as i:
                    for u in range(U):
                        pool.wait_ge(idx_ready[u], (i + turn * NU) * 16 + 16)
                        pool.wait_ge(used, (i - 1) * U + (u + 1))
                        pool.nop(nofuse=True)
                        gather(table, slots, u)

            pool.wait_ge(up_saved, 16 * NCH)
            gather_pass(0, up_tab, rows, prod_ready)
            pool.wait_ge(max_ready, 1)
            pool.partition_all_reduce(s_max[:, 1, :], s_max[:, 0, :], P, bass.bass_isa.ReduceOp.max).then_inc(max_all, 1)
            pool.wait_ge(scores_saved, 48)
            gather_pass(1, score_tab, s_rows, z_ready)
            pool.wait_ge(xh_saved, 16)
            gather_pass(2, xh_tab, rows, weighed_ready)

        @block.scalar
        def _(act):
            def up_chunk(c, first):
                act.wait_ge(up_done, c + 1)
                if not first:
                    act.wait_ge(up_saved, c * 16)
                act.activation(node_a[:, 0:4, :], bank[0][:, :].rearrange("p (b f) -> p b f", f=D), ACT.Copy,
                               scale=INV_UP).then_inc(up_copied, 1)
                act.activation(node_a[:, 4:7, :], bank[1][:, 0:3 * D].rearrange("p (b f) -> p b f", f=D), ACT.Copy,
                               scale=INV_UP).then_inc(up_copied, 1)
                act.wait_ge(up_copied, c * 2 + 2)
                act.dma_start(up_tab[bass.ds(c * CN, CN), :].rearrange("(b p) f -> p b f", p=P),
                              node_a[:, :, :]).then_inc(up_saved, 16)

            up_chunk(0, True)
            with act.Fori(1, NCH) as c:
                up_chunk(c, False)

            def silu1(g, s):
                act.wait_ge(l1_done, g + 1)
                act.activation(h1[:, s, :], p_h[s][:, 0, :], ACT.Silu, bias=b1_sb[:, 0:1]).then_inc(h1_ready, 1)

            def silu2(g, s):
                act.wait_ge(l2_done, g + 1)
                act.activation(h2[:, s, :], p_h[s][:, 1, :], ACT.Silu, bias=b2_sb[:, 0:1]).then_inc(h2_ready, 1)

            silu1(0, 0)
            silu2(0, 0)
            silu1(1, 1)
            with act.Fori(0, NG // 2) as i:
                for u in range(2):
                    silu2(i * 2 + (u + 1), (u + 1) % 2)
                    silu1(i * 2 + (u + 2), u)

            with act.Fori(0, NCH) as c:
                act.wait_ge(out_t_done, c + 1)
                for h in range(2):
                    act.activation(chunk[:, h * CN // 2:(h + 1) * CN // 2], bank[h][:, 0:CN // 2], ACT.Copy
                                   ).then_inc(out_t_copied, 1)
                act.wait_ge(var_ready, c + 1)
                act.activation(node_s[:, 2, :], node_s[:, 1, :], ACT.Sqrt).then_inc(std_ready, 1)
                act.wait_ge(x1_t_done, c + 1)
                act.activation(chunk[:, 0:4 * P], bank[4][:, :], ACT.Copy).then_inc(x1_t_copied, 1)
                act.activation(chunk[:, 4 * P:CN], bank[5][:, 0:3 * P], ACT.Copy).then_inc(x1_t_copied, 1)
                act.wait_ge(xh_done, c + 1)
                for b in range(0, CB, 3):
                    n = min(3, CB - b)
                    src = bank[(6 + b // 3) % 8][:, 0:n * XW].rearrange("p (b f) -> p b f", f=XW)
                    act.activation(xh[:, bass.ds(c * CB + b, n), :], src[:, :, 0:D], ACT.Copy)
                    act.activation(score[:, bass.ds(c * CB + b, n), :], src[:, :, D:XW], ACT.Copy).then_inc(xh_copied, 1)

            with act.Fori(0, NG // 2) as i:
                for u in range(2):
                    act.wait_ge(z_ready, i * 2 + (u + 1))
                    act.activation(ex[:, bass.ds((i * 2 + u) * TG, TG), :], z[:, u, :, :], ACT.Exp).then_inc(ex_ready, 1)

            def nodes1(c, first):
                if not first:
                    act.wait_ge(last_done, c)
                act.activation(chunk[:, :], acc1[:, bass.ds(c * CN, CN)], ACT.Copy).then_inc(last_copied, 1)
                for n in range(2):
                    act.wait_ge(last_var, c * 2 + (n + 1))
                    act.activation(node_s[:, 2, :], node_s[:, 1, :], ACT.Sqrt).then_inc(last_std, 1)

            act.wait_ge(agg_ready, 1)
            nodes1(0, True)
            with act.Fori(1, NCH) as c:
                nodes1(c, False)

        @block.tensor
        def _(pe):
            def up_chunk(c, first):
                pe.wait_ge(xt_loaded, c * 16 + 16)
                if not first:
                    pe.wait_ge(up_copied, c * 2)
                for b in range(CB):
                    mm = nc.tensor.matmul(blocks(0, b, D), chunk[:, b * P:(b + 1) * P], w_up[:, :], start=True, stop=True)
                mm.then_inc(up_done, 1)

            pe.wait_ge(loaded, 16 * N_LOADS)
            up_chunk(0, True)
            with pe.Fori(1, NCH) as c:
                up_chunk(c, False)
            pe.wait_ge(up_copied, 2 * NCH)

            def layer1(g, s, u, use):
                pe.wait_ge(ea_ready[u], use * 16 + 16)
                nc.tensor.matmul(p_h[s][:, 0, :], a1_sb[:, :], ea[:, u, :], start=True, stop=True).then_inc(l1_done, 1)

            def layer2(g, s):
                pe.wait_ge(h1_ready, g + 1)
                nc.tensor.matmul(p_h[s][:, 1, :], a2_sb[:, :], h1[:, s, :], start=True, stop=True).then_inc(l2_done, 1)

            def layer3(g, s):
                pe.wait_ge(h2_ready, g + 1)
                for j in range(2):
                    mm = nc.tensor.matmul(p_w[s][:, 2 * j:2 * j + 2, :], h2[:, s, P * j:P * (j + 1)], a3_sb[:, :],
                                          start=True, stop=True)
                mm.then_inc(w_done, 1)

            def segment_sum(dst_ps, s):
                for k in range(TG):
                    nc.tensor.matmul(dst_ps[:, 0, :], prod[:, s, k, 0, :], sel[:, s, k, 0, :],
                                     start=(k == 0), stop=(k == TG - 1))
                for k in range(TG):
                    mm = nc.tensor.matmul(dst_ps[:, 1:4, :], prod[:, s, k, 1, :], sel[:, s, k, 1:4, :],
                                          start=(k == 0), stop=(k == TG - 1))
                return mm

            def further_windows(g, body):
                x0 = pe.value_load(g_tab[0:1, 1, bass.ds(g, 1)], min_val=0, max_val=XMAX)
                x1 = pe.value_load(g_tab[0:1, 1, bass.ds(g + 1, 1)], min_val=0, max_val=XMAX)
                with pe.If(x1 > x0):
                    with pe.Fori(x0, x1) as x:
                        body(x)

            def further_sums(s):
                def body(x):
                    pe.wait_ge(selx_ready, x + 1)
                    segment_sum(p_segx, s).then_inc(segx_done, 1)
                return body

            def step_a(i, u, first):
                g, s = i * U + u, u % 2
                layer3(g, s)
                layer2(g + 1, 1 - s)
                layer1(g + 2, s, (u + 2) % U, i + (u + 2) // U)
                pe.wait_ge(prod_ready, g + 1)
                segment_sum(p_seg[s], s).then_inc(seg_done, 1)
                if not first:
                    further_windows(g - 1, further_sums(1 - s))

            pe.wait_ge(table_ready, 1)
            layer1(0, 0, 0, 0)
            layer1(1, 1, 1, 0)
            layer2(0, 0)
            for u in range(U):
                step_a(0, u, u == 0)
            with pe.Fori(1, NU) as i:
                for u in range(U):
                    step_a(i, u, False)
            further_windows(NG - 1, further_sums((NG - 1) % 2))

            def nodes0(c, first):
                if not first:
                    pe.wait_ge(xh_copied, c * 3)
                for h in range(2):
                    for k in range(4):
                        mm = nc.tensor.matmul(bank[h][:, 0:CN // 2], w_out[:, k, :],
                                              acc0[:, k, bass.ds(c * CN + h * CN // 2, CN // 2)],
                                              start=(k == 0), stop=(k == 3))
                mm.then_inc(out_t_done, 1)
                pe.wait_ge(out_t_copied, c * 2 + 2)
                for b in range(CB):
                    mm = nc.tensor.transpose(blocks(2, b, P), chunk[:, b * P:(b + 1) * P], ident[:, :])
                mm.then_inc(out_done, 1)
                pe.wait_ge(x1_ready, c + 1)
                for b in range(CB):
                    mm = nc.tensor.transpose(blocks(4, b, P), node_a[:, b, :], ident[:, :])
                mm.then_inc(x1_t_done, 1)
                pe.wait_ge(x1_t_copied, c * 2 + 2)
                for b in range(CB):
                    mm = nc.tensor.matmul(blocks(6, b, XW), chunk[:, b * P:(b + 1) * P], w_cat[:, :], start=True, stop=True)
                mm.then_inc(xh_done, 1)

            pe.wait_ge(sums_ready, 1)
            pe.wait_ge(h1_ready, NG + 2)
            pe.wait_ge(h2_ready, NG + 1)
            nodes0(0, True)
            with pe.Fori(1, NCH) as c:
                nodes0(c, False)

            pe.wait_ge(hist_zero, 1)
            nc.tensor.matmul(p_den, ident[:, :], hist_rhs[:, 0, 0, :, :], start=True, stop=False).then_inc(hist_start, 1)

            def receivers(dst_ps, s, win):
                for k in range(TG):
                    mm = nc.tensor.matmul(dst_ps[:, k, :], sel_t[:, s, k * P:(k + 1) * P], win, start=True, stop=True)
                return mm

            def histogram(g, s, last=False):
                pe.wait_ge(hist_ready, g + 1)
                for k in range(TG):
                    mm = nc.tensor.matmul(p_den, lo_hot[:, s, k, :], hist_rhs[:, s, k, :, :], start=False,
                                          stop=last and k == TG - 1)
                mm.then_inc(hist_done, 1)

            def further_receivers(s):
                def body(x):
                    pe.wait_ge(sjx_ready, x * 16 + 16)
                    pe.wait_ge(sel_tx_ready, x + 1)
                    receivers(p_sjx, s, sj_winx[:, :]).then_inc(sjx_done, 1)
                return body

            def step_b(i, u, first):
                g, s = i * U + u, u % 2
                pe.wait_ge(sj_ready[u], i * 16 + 16)
                pe.wait_ge(sel_t_ready, g + 1)
                receivers(p_sj[s], s, sj_win[:, u, :]).then_inc(sj_done, 1)
                if not first:
                    histogram(g - 1, 1 - s)
                further_windows(g, further_receivers(s))

            for u in range(U):
                step_b(0, u, u == 0)
            with pe.Fori(1, NU) as i:
                for u in range(U):
                    step_b(i, u, False)
            histogram(NG - 1, (NG - 1) % 2, True)

            def aggregate(dst_ps, s):
                for k in range(TG):
                    mm = nc.tensor.matmul(dst_ps[:, 0, :], weighed[:, s, k, :], sel[:, s, k, 0, :],
                                          start=(k == 0), stop=(k == TG - 1))
                return mm

            def further_aggregates(s):
                def body(x):
                    pe.wait_ge(hotx_ready, x + 1)
                    aggregate(p_segx, s).then_inc(aggx_done, 1)
                return body

            def step_c(i, u, first):
                g, s = i * U + u, u % 2
                pe.wait_ge(weighed_ready, g + 1)
                aggregate(p_seg[s], s).then_inc(agg_done, 1)
                if not first:
                    further_windows(g - 1, further_aggregates(1 - s))

            for u in range(U):
                step_c(0, u, u == 0)
            with pe.Fori(1, NU) as i:
                for u in range(U):
                    step_c(i, u, False)
            further_windows(NG - 1, further_aggregates((NG - 1) % 2))

            def nodes1(c, first):
                pe.wait_ge(last_copied, c + 1)
                if not first:
                    pe.wait_ge(last_var, c * 2)
                for b in range(CB):
                    mm = nc.tensor.transpose(blocks(2, b, P), chunk[:, b * P:(b + 1) * P], ident[:, :])
                mm.then_inc(last_done, 1)

            nodes1(0, True)
            with pe.Fori(1, NCH) as c:
                nodes1(c, False)

        @block.vector
        def _(dve):
            V = nc.vector
            for n, tile in enumerate((w_up[:, :], a1_sb[:, :], a2_sb[:, :], a3_sb[:, :], w_out[:, :, :])):
                V.memset(tile, 0.0).then_inc(cleared, 1)
            V.memset(zeros[:, :], 0.0)

            steps = [0]

            def link(ins):
                steps[0] += 1
                ins.then_inc(prep, 1)
                dve.wait_ge(prep, steps[0])

            dve.wait_ge(rng_loaded, 16)
            link(V.tensor_reduce(rng_f[:, 0, :], rng_i, AX.X, ALU.min))
            link(V.tensor_reduce(rng_f[:, 1, :], rng_i, AX.X, ALU.max))
            link(V.tensor_tensor(rng_f[:, 2, :], rng_f[:, 1, :], rng_f[:, 0, :], ALU.subtract))
            link(V.tensor_copy(rng_o[:, 1, :], rng_f[:, 2, :]))
            link(V.tensor_copy(rng_o[:, 0, :], rng_f[:, 0, :]))
            V.tensor_scalar(rng_o[:, 1, :], rng_o[:, 1, :], W.bit_length() - 1, None, ALU.arith_shift_right
                            ).then_inc(rng_ready, 1)
            link(V.memset(acc[:, :], 0.0))
            dve.wait_ge(dst_loaded, 16)
            V.tensor_copy(dst_sb[:, :], tile_i[:, :]).then_inc(tile_free, 1)
            dve.wait_ge(tile_free, 1)
            dve.wait_ge(rng_back, 16)
            link(V.tensor_copy(g_sum[:, 0, :], g_tab[:, 1, 0:NG]))
            now, d = 0, 1
            while d < NG:
                V.tensor_copy(g_sum[:, 1 - now, 0:d], g_sum[:, now, 0:d]).then_inc(prep, 1)
                steps[0] += 1
                link(V.tensor_tensor(g_sum[:, 1 - now, d:NG], g_sum[:, now, d:NG], g_sum[:, now, 0:NG - d], ALU.add))
                now, d = 1 - now, 2 * d
            link(V.memset(g_tab[:, 1, 0:1], 0))
            link(V.tensor_copy(g_tab[:, 1, 1:NG + 1], g_sum[:, now, :]))
            dve.wait_ge(loaded, 16 * N_LOADS)
            link(V.tensor_scalar(w_out[:, :, :], w_out[:, :, :], INV_OUT, None, ALU.mult))
            for i in range(3):
                r = slice(MUL * (1 + i), MUL * (2 + i))
                link(V.tensor_scalar(w_out[r, 1 + i, :], w_out[r, 1 + i, :], INV_R3, None, ALU.mult))
            a_prod = node_b[:, 0:2, :].rearrange("p q (h j) -> p q h j", h=HEADS)
            for q in range(2):
                link(V.tensor_tensor(a_prod[:, q], w_cat[:, 0:D].rearrange("p (h j) -> p h j", h=HEADS),
                                     a_bc[:, :, q * HD:(q + 1) * HD], ALU.mult))
                link(V.tensor_reduce(w_cat[:, D + q * HEADS:D + (q + 1) * HEADS], a_prod[:, q], AX.X, ALU.add))
            dve.wait_ge(consts, 4)
            dve.sem_inc(summedx, 1)
            dve.sem_inc(addedx, 1)
            dve.sem_inc(z_sumx, 1)
            dve.sem_inc(table_ready, 1)

            def load_range(g):
                return (dve.value_load(g_tab[0:1, 0, bass.ds(g, 1)], min_val=0, max_val=NP - 1),
                        dve.value_load(g_tab[0:1, 1, bass.ds(g, 1)], min_val=0, max_val=XMAX),
                        dve.value_load(g_tab[0:1, 1, bass.ds(g + 1, 1)], min_val=0, max_val=XMAX))

            def further_windows(rng, body):
                base, x0, x1 = rng
                with dve.If(x1 > x0):
                    with dve.Fori(x0, x1) as x:
                        body(x, window(base, x, x0))

            carried = [None]

            def select(g, s, base):
                for k in range(TG):
                    ins = V.scalar_tensor_tensor(
                        sel[:, s, k, :, :], iota_n[:, bass.ds(base, W)].unsqueeze(1).to_broadcast([P, 4, W]),
                        dst_sb[:, bass.ds(g * TG + k, 1)],
                        y_sb[:, bass.ds(g * TG + k, 1), :].rearrange("p o c -> p (o c)").unsqueeze(2).to_broadcast([P, 4, W]),
                        ALU.is_equal, ALU.mult)
                return ins

            def add_sums(ps, at0):
                cols = acc0[:, :, bass.ds(at0, W)]
                return V.tensor_tensor(cols, cols, ps, ALU.add)

            def flush_a(g, s, first, rng):
                base, x0, _ = rng
                dve.wait_ge(seg_done, g + 1)
                if not first:
                    dve.wait_ge(summed, g)
                dve.wait_ge(summedx, x0 + 1)
                add_sums(p_seg[s], base).then_inc(summed, 1)

                def body(x, at0):
                    select(g, s, at0).then_inc(selx_ready, 1)
                    dve.wait_ge(segx_done, x + 1)
                    dve.wait_ge(summed, g + 1)
                    dve.wait_ge(summedx, x + 1)
                    add_sums(p_segx, at0).then_inc(summedx, 1)

                further_windows(rng, body)

            def step_a(i, u, n):
                g, s = i * U + u, u % 2
                if u == 0 and n > 0:
                    carried[0] = load_range(g - 1)
                rng = load_range(g)
                select(g, s, rng[0])
                dve.wait_ge(gathered[u], i * (16 * TG) + 16 * TG)
                dve.wait_ge(w_done, g + 1)
                s_rows0 = rows[:, u, :, 0:MUL].unsqueeze(2).to_broadcast([P, TG, 2, MUL])
                w4 = p_w[s].rearrange("p k (q m) -> p k q m", q=4)
                V.tensor_tensor(prod[:, s, :, :, 0:MUL], s_rows0, w4[:, :, 0:2, :], ALU.mult)
                v_rows = rows[:, u, :, MUL:D].rearrange("p k (i m) -> p k i m", i=3)
                for q in range(2):
                    ins = V.tensor_tensor(prod[:, s, :, q, MUL:D].rearrange("p k (i m) -> p k i m", i=3), v_rows,
                                          w4[:, :, 2 + q, :].unsqueeze(2).to_broadcast([P, TG, 3, MUL]), ALU.mult)
                ins.then_inc(prod_ready, 1)
                if n > 0:
                    flush_a(g - 1, 1 - s, n == 1, carried[0])
                carried[0] = rng

            for u in range(U):
                step_a(0, u, u)
            with dve.Fori(1, NU) as i:
                for u in range(U):
                    step_a(i, u, U)
            flush_a(NG - 1, (NG - 1) % 2, False, load_range(NG - 1))
            dve.wait_ge(summed, NG)
            all_x = dve.value_load(g_tab[0:1, 1, NG:NG + 1], min_val=0, max_val=XMAX)
            dve.wait_ge(summedx, all_x + 1)
            dve.sem_inc(sums_ready, 1)

            def centre(tile, sq, count, at_step, var_sem):
                def chain(k, ins):
                    ins.then_inc(count, 1)
                    dve.wait_ge(count, at_step + k)
                chain(1, V.tensor_reduce(node_s[:, 0, :], tile, AX.X, ALU.add))
                chain(2, V.tensor_scalar(node_s[:, 0, :], node_s[:, 0, :], 1.0 / D, None, ALU.mult))
                chain(3, V.tensor_tensor(tile, tile, node_s[:, 0, :].unsqueeze(2).to_broadcast([P, CB, D]), ALU.subtract))
                chain(4, V.tensor_tensor(sq, tile, tile, ALU.mult))
                chain(5, V.tensor_reduce(node_s[:, 1, :], sq, AX.X, ALU.add))
                V.tensor_scalar(node_s[:, 1, :], node_s[:, 1, :], 1.0 / D, EPS, ALU.mult, ALU.add).then_inc(var_sem, 1)

            def scale_rows(tile, count, at_step, std_sem, std_count):
                dve.wait_ge(std_sem, std_count)
                V.reciprocal(node_s[:, 3, :], node_s[:, 2, :]).then_inc(count, 1)
                dve.wait_ge(count, at_step + 6)
                return V.tensor_tensor(tile, tile, node_s[:, 3, :].unsqueeze(2).to_broadcast([P, CB, D]), ALU.mult)

            def v_nodes(tile):
                return tile.rearrange("p b (m i) -> p b m i", i=3)

            def nodes0(c, first):
                dve.wait_ge(xn_loaded, c * 16 + 16)
                dve.wait_ge(out_done, c + 1)
                if not first:
                    dve.wait_ge(x1_saved, c * 16)
                for first_b, n in ((0, 4), (4, 3)):
                    ps = bank[2 + first_b // 4][:, 0:n * P].rearrange("p (b f) -> p b f", f=P)
                    r = slice(first_b, first_b + n)
                    V.tensor_tensor(node_a[:, r, 0:MUL], node_b[:, r, 0:MUL], ps[:, :, 0:MUL], ALU.add).then_inc(node, 1)
                    V.tensor_tensor(v_nodes(node_a[:, r, MUL:D]), v_nodes(node_b[:, r, MUL:D]),
                                    ps[:, :, MUL:D].rearrange("p b (i m) -> p b m i", i=3), ALU.add).then_inc(node, 1)
                dve.wait_ge(node, c * 10 + 4)
                centre(node_a[:, :, :], scratch, node, c * 10 + 4, var_ready)
                scale_rows(node_a[:, :, :], node, c * 10 + 4, std_ready, c + 1).then_inc(x1_ready, 1)

            nodes0(0, True)
            with dve.Fori(1, NCH) as c:
                nodes0(c, False)

            dve.wait_ge(xh_copied, 3 * NCH)
            V.tensor_reduce(s_max[:, 0, :], score[:, :, HEADS:].rearrange("p b h -> p h b"), AX.X, ALU.max
                            ).then_inc(max_ready, 1)
            dve.wait_ge(src_loaded, 16)
            dve.wait_ge(x1_t_done, NCH)
            n0 = steps[0]
            V.tensor_scalar(int_lo, tile_i[:, :], P - 1, None, ALU.bitwise_and).then_inc(prep, 1)
            V.tensor_scalar(int_hi, tile_i[:, :], P.bit_length() - 1, None, ALU.arith_shift_right).then_inc(prep, 1)
            steps[0] += 2
            dve.wait_ge(prep, steps[0])
            V.tensor_copy(src_lo, int_lo).then_inc(prep, 1)
            V.tensor_copy(src_hi, int_hi).then_inc(prep, 1)
            V.memset(acc1, 0.0).then_inc(prep, 1)
            steps[0] += 3
            dve.wait_ge(prep, steps[0])
            V.memset(hist_rhs[:, 0, 0, :, :], 0.0).then_inc(hist_zero, 1)
            dve.wait_ge(max_all, 1)
            link(V.tensor_copy(shift[:, :, 0:HEADS], score[:, :, 0:HEADS]))
            link(V.tensor_tensor(shift[:, :, HEADS:], score[:, :, 0:HEADS],
                                 s_max[:, 1, :].unsqueeze(1).to_broadcast([P, NB, HEADS]), ALU.add))
            V.scalar_tensor_tensor(shift[:, :, HEADS:], shift[:, :, HEADS:], ALPHA, shift[:, :, HEADS:], ALU.mult, ALU.max
                                   ).then_inc(shift_ready, 1)
            dve.wait_ge(hist_start, 1)

            def select_t(u, s, at0):
                return V.tensor_scalar(sel_t[:, s, :], dst_row[:, u, :], p_col[0:W, 0:1], iota_n[0:W, bass.ds(at0, 1)],
                                       ALU.subtract, ALU.is_equal)

            def hist_operands(g, s):
                dve.wait_ge(ex_ready, g + 1)
                for k in range(TG):
                    ins = V.scalar_tensor_tensor(
                        hist_rhs[:, s, k, :, :], iota_n[:, 0:NB].unsqueeze(2).to_broadcast([P, NB, HEADS]),
                        src_hi[:, bass.ds(g * TG + k, 1)],
                        ex[:, bass.ds(g * TG + k, 1), :].to_broadcast([P, NB, HEADS]), ALU.is_equal, ALU.mult)
                ins.then_inc(hist_ready, 1)

            def step_b(i, u, n):
                g, s = i * U + u, u % 2
                rng = load_range(g)
                dve.wait_ge(row_ready[u], i * 16 + 16)
                select_t(u, s, rng[0]).then_inc(sel_t_ready, 1)
                if n > 0:
                    hist_operands(g - 1, 1 - s)
                if n > 1:
                    dve.wait_ge(hist_done, g - 1)
                V.tensor_tensor(lo_hot[:, s, :, :], iota_n[:, 0:P].unsqueeze(1).to_broadcast([P, TG, P]),
                                src_lo[:, bass.ds(g * TG, TG)].unsqueeze(2).to_broadcast([P, TG, P]), ALU.is_equal)
                dve.wait_ge(gathered[u], (i + NU) * (16 * TG) + 16 * TG)
                dve.wait_ge(sj_done, g + 1)
                V.tensor_tensor(z[:, 2, :, :], s_rows[:, u, :, 0:HEADS], p_sj[s], ALU.add).then_inc(z_sum, 1)

                def body(x, at0):
                    select_t(u, s, at0).then_inc(sel_tx_ready, 1)
                    dve.wait_ge(sjx_done, x + 1)
                    dve.wait_ge(z_sum, g + 1)
                    dve.wait_ge(z_sumx, x + 1)
                    V.tensor_tensor(z[:, 2, :, :], z[:, 2, :, :], p_sjx, ALU.add).then_inc(z_sumx, 1)

                further_windows(rng, body)
                dve.wait_ge(z_sum, g + 1)
                dve.wait_ge(z_sumx, rng[2] + 1)
                V.scalar_tensor_tensor(z[:, 2, :, :], z[:, 2, :, :], ALPHA, z[:, 2, :, :], ALU.mult, ALU.max).then_inc(leaky, 1)
                dve.wait_ge(leaky, g + 1)
                V.tensor_tensor(z[:, s, :, :], z[:, 2, :, :], s_rows[:, u, :, HEADS:], ALU.subtract).then_inc(z_ready, 1)

            for u in range(U):
                step_b(0, u, u)
            with dve.Fori(1, NU) as i:
                for u in range(U):
                    step_b(i, u, U)
            hist_operands(NG - 1, (NG - 1) % 2)

            dve.wait_ge(hist_done, NG)
            d_ps = p_den.rearrange("p (b h) -> p b h", h=HEADS)
            link(V.tensor_scalar(den[:, 0, :, :], d_ps, 0.0, None, ALU.is_equal))
            link(V.tensor_tensor(den[:, 1, :, :], den[:, 0, :, :], d_ps, ALU.add))
            link(V.reciprocal(den[:, 0, :, :], den[:, 1, :, :]))
            xh_heads = yx[:, 0:NB * D].rearrange("p (q j) -> p q j", j=HD)
            V.tensor_tensor(xh_heads, xh_heads,
                            den[:, 0, :, :].rearrange("p b h -> p (b h)").unsqueeze(2).to_broadcast([P, NB * HEADS, HD]),
                            ALU.mult).then_inc(xh_ready, 1)

            def one_hot(g, s, at0):
                return V.tensor_tensor(sel[:, s, :, 0, :], iota_n[:, bass.ds(at0, W)].unsqueeze(1).to_broadcast([P, TG, W]),
                                       dst_sb[:, bass.ds(g * TG, TG)].unsqueeze(2).to_broadcast([P, TG, W]), ALU.is_equal)

            def add_aggregate(ps, at0):
                cols = acc1[:, bass.ds(at0, W)]
                return V.tensor_tensor(cols, cols, ps[:, 0, :], ALU.add)

            def flush_c(g, s, first, rng):
                base, x0, _ = rng
                dve.wait_ge(agg_done, g + 1)
                if not first:
                    dve.wait_ge(added, g)
                dve.wait_ge(addedx, x0 + 1)
                add_aggregate(p_seg[s], base).then_inc(added, 1)

                def body(x, at0):
                    one_hot(g, s, at0).then_inc(hotx_ready, 1)
                    dve.wait_ge(aggx_done, x + 1)
                    dve.wait_ge(added, g + 1)
                    dve.wait_ge(addedx, x + 1)
                    add_aggregate(p_segx, at0).then_inc(addedx, 1)

                further_windows(rng, body)

            def step_c(i, u, n):
                g, s = i * U + u, u % 2
                if u == 0 and n > 0:
                    carried[0] = load_range(g - 1)
                rng = load_range(g)
                one_hot(g, s, rng[0])
                dve.wait_ge(gathered[u], (i + 2 * NU) * (16 * TG) + 16 * TG)
                V.tensor_tensor(weighed[:, s, :, :].rearrange("p k (h j) -> p k h j", h=HEADS),
                                rows[:, u, :, :].rearrange("p k (h j) -> p k h j", h=HEADS),
                                ex[:, bass.ds(g * TG, TG), :].unsqueeze(3).to_broadcast([P, TG, HEADS, HD]),
                                ALU.mult).then_inc(weighed_ready, 1)
                if n > 0:
                    flush_c(g - 1, 1 - s, n == 1, carried[0])
                carried[0] = rng

            for u in range(U):
                step_c(0, u, u)
            with dve.Fori(1, NU) as i:
                for u in range(U):
                    step_c(i, u, U)
            flush_c(NG - 1, (NG - 1) % 2, False, load_range(NG - 1))
            dve.wait_ge(added, NG)
            all_x = dve.value_load(g_tab[0:1, 1, NG:NG + 1], min_val=0, max_val=XMAX)
            dve.wait_ge(addedx, all_x + 1)
            dve.sem_inc(agg_ready, 1)

            LAST = 18

            def nodes1(c, first):
                at0 = c * LAST
                dve.wait_ge(x1_loaded, c * 16 + 16)
                dve.wait_ge(last_done, c + 1)
                if not first:
                    dve.wait_ge(out_saved, c * 16)
                for first_b, n in ((0, 4), (4, 3)):
                    ps = bank[2 + first_b // 4][:, 0:n * P].rearrange("p (b f) -> p b f", f=P)
                    r = slice(first_b, first_b + n)
                    V.tensor_tensor(node_a[:, r, :], node_b[:, r, :], ps, ALU.add).then_inc(last, 1)
                dve.wait_ge(last, at0 + 2)
                centre(node_a[:, :, :], scratch, last, at0 + 2, last_var)
                scale_rows(node_a[:, :, :], last, at0 + 2, last_std, c * 2 + 1).then_inc(last, 1)
                dve.wait_ge(last, at0 + 9)
                tile = node_a[:, :, :]
                V.tensor_tensor(tile, tile, gamma_bc[:, :].unsqueeze(1).to_broadcast([P, CB, D]), ALU.mult).then_inc(last, 1)
                dve.wait_ge(last, at0 + 10)
                V.tensor_tensor(tile, tile, beta_bc[:, :].unsqueeze(1).to_broadcast([P, CB, D]), ALU.add).then_inc(last, 1)
                dve.wait_ge(last, at0 + 11)
                V.tensor_tensor(tile, tile, node_b[:, :, :], ALU.add).then_inc(last, 1)
                dve.wait_ge(last, at0 + 12)
                centre(node_a[:, :, :], scratch, last, at0 + 12, last_var)
                scale_rows(node_a[:, :, :], last, at0 + 12, last_std, c * 2 + 2).then_inc(y_ready, 1)

            nodes1(0, True)
            with dve.Fori(1, NCH) as c:
                nodes1(c, False)


def _pad(a, n, fill):
    import numpy as np
    return np.concatenate([a, np.full((n - a.shape[0],) + a.shape[1:], fill, a.dtype)])


def kernel(**inputs):
    import numpy as np
    import concourse.bacc as bacc
    from concourse.bass_utils import run_bass_kernel_spmd as run

    a = {k: np.asarray(v) for k, v in inputs.items()}
    ep = NG * GE
    x = _pad(a["x"], NP + CN, 0)
    comp_major = np.concatenate([np.arange(MUL)] + [MUL + 3 * np.arange(MUL) + i for i in range(3)])
    src = _pad(a["src"], ep, NP - 1)
    dst = _pad(a["dst"], ep, NP - 1)
    y = _pad(a["edge_attr_4"], ep, 0)
    ea = _pad(a["edge_attr_8"], ep + 2 * GE, 0)
    arrays = {
        "x_t": x[:NP, comp_major].T,
        "x_n": x,
        "src_t": src.reshape(T, P).T,
        "src_g": src.reshape(NG, TG, P).transpose(0, 2, 1).reshape(NG * P, TG),
        "dst_t": dst.reshape(T, P).T,
        "dst_f": dst.reshape(NG, GE),
        "y_t": y.reshape(T, P, 4).transpose(1, 0, 2).reshape(P, T * 4),
        "ea_t": ea.reshape(NG + 2, 2, 2, P, EF).transpose(2, 4, 0, 1, 3).reshape(2 * EF, (NG + 2) * HG),
        "w_up_s": a["L0_gnn_W_up_s"], "w_up_v": a["L0_gnn_W_up_v"],
        "a1": a["L0_gnn_A1"], "b1": a["L0_gnn_b1"], "a2": a["L0_gnn_A2"], "b2": a["L0_gnn_b2"], "a3": a["L0_gnn_A3"],
        "w_out_s": a["L0_gnn_W_out_s"], "w_out_v": a["L0_gnn_W_out_v"],
        "w_att": a["L1_gnn_W"], "a_att": a["L1_gnn_a"].reshape(HEADS * 2 * HD),
        "gamma": a["L1_gnn_ln_gamma"], "beta": a["L1_gnn_ln_beta"],
    }
    arrays = {k: np.ascontiguousarray(v) for k, v in arrays.items()}
    nc = bacc.Bacc("TRN2", target_bir_lowering=False, num_devices=1)
    args = {k: nc.dram_tensor(k, v.shape, mybir.dt.from_np(v.dtype), kind="ExternalInput").ap() for k, v in arrays.items()}
    args["out"] = nc.dram_tensor("out", (NP, D), F32, kind="ExternalOutput").ap()
    for name, shape, dt in (("up_tab", (NP, D), F32), ("x1_tab", (NP, D), F32), ("score_tab", (NP, 2 * HEADS), F32),
                            ("sj_tab", (NW, HEADS), F32), ("xh_tab", (NP, D), F32), ("range_tab", (2, NG), I32)):
        args[name] = nc.dram_tensor(name, shape, dt, kind="Internal").ap()
    build(nc, **args)
    return run(nc, [arrays], core_ids=[0]).results[0]["out"][:N_NODES]
```
